# Optimizing a Trainium2 kernel written in Bass

```python
import numpy as np
import jax
import jax.numpy as jnp

def _softmax(x, axis=-1):
    return jax.nn.softmax(x, axis=axis)

def _gelu(x):
    return jax.nn.gelu(x, approximate=True)

def _silu(x):
    return jax.nn.silu(x)

def _sigmoid(x):
    return jax.nn.sigmoid(x)

def _layernorm(x, axis=-1, eps=1e-05):
    m = jnp.mean(x, axis=axis, keepdims=True)
    v = jnp.var(x, axis=axis, keepdims=True)
    return (x - m) / jnp.sqrt(v + eps)

def _scatter_add(tgt, idx, src, axis=0):
    return tgt.at[idx].add(src)

def _segment_sum(src, seg, n):
    return jax.ops.segment_sum(src, seg, n)
kernel_name = 'mk_gnn_resnorm_d2_gnn_r32_cf1a9b'

def setup_inputs(seed: int=0):
    np.random.seed(seed)
    _w = jnp.asarray

    def _rec_inputs():
        import jax
        import jax.numpy as jnp
        _gk = jax.random.key(seed)
        x = -0.0003713 + 1 * jax.random.normal(jax.random.fold_in(_gk, 1), (3125, 128), jnp.float32)
        src = jax.random.randint(jax.random.fold_in(_gk, 2), (100000,), 0, 3125, jnp.int32)
        dst = jnp.minimum((3125 * jax.random.uniform(jax.random.fold_in(_gk, 3), (100000,)) ** 2.0).astype(jnp.int32), 99999)
        _o = jnp.argsort(dst, stable=True)
        src = src[_o]
        dst = dst[_o]
        return (x, src, dst)
    x, src, dst = _rec_inputs()

    def _L0_gnn_setup():
        import jax, jax.numpy as jnp
        import numpy as np
        N_NODES = 3125
        N_EDGES = 50000
        D_IN = 128
        D_HID = 128
        D_OUT = 128

        def _sage_conv(x, src, dst, W_l, b_l, W_r):
            msg = x[src]
            summed = jax.ops.segment_sum(msg, dst, num_segments=N_NODES)
            cnt = jax.ops.segment_sum(jnp.ones((src.shape[0],), x.dtype), dst, num_segments=N_NODES)
            aggr = summed / jnp.maximum(cnt, 1.0)[:, None]
            return aggr @ W_l + b_l + x @ W_r
        key = jax.random.key(seed)
        ks = jax.random.split(key, 8)
        x = jax.random.normal(ks[0], (N_NODES, D_IN), dtype=jnp.float32)
        edge_index = jax.random.randint(ks[1], (2, N_EDGES), 0, N_NODES, dtype=jnp.int32)
        s = 1.0 / np.sqrt(D_IN)
        W_l0 = jax.random.uniform(ks[2], (D_IN, D_HID), jnp.float32, -s, s)
        b_l0 = jnp.zeros((D_HID,), jnp.float32)
        W_r0 = jax.random.uniform(ks[3], (D_IN, D_HID), jnp.float32, -s, s)
        W_l1 = jax.random.uniform(ks[4], (D_HID, D_OUT), jnp.float32, -s, s)
        b_l1 = jnp.zeros((D_OUT,), jnp.float32)
        W_r1 = jax.random.uniform(ks[5], (D_HID, D_OUT), jnp.float32, -s, s)
        return {'x': x, 'edge_index': edge_index, 'W_l0': W_l0, 'b_l0': b_l0, 'W_r0': W_r0, 'W_l1': W_l1, 'b_l1': b_l1, 'W_r1': W_r1}
    _L0_gnn_all = _L0_gnn_setup()
    _L0_gnn_in = {k: v for k, v in _L0_gnn_all.items() if k in ('W_l0', 'b_l0', 'W_r0', 'W_l1', 'b_l1', 'W_r1')}
    del _L0_gnn_all

    def _L1_gnn_setup():
        import jax, jax.numpy as jnp
        import numpy as np
        TOPK = 2
        key = jax.random.key(seed)
        ks = jax.random.split(key, 18)
        N, E = (625, 10000)
        IN, H, OUT, L = (128, 256, 128, 3)
        NW, NS = (4, 4)
        NE = NW + NS

        def w(k, shape, fan):
            return jax.random.normal(k, shape, dtype=jnp.float32) / np.float32(np.sqrt(fan))
        inp = {'x': jax.random.normal(ks[0], (N, IN), dtype=jnp.float32), 'edge_index': jax.random.randint(ks[1], (2, E), 0, N, dtype=jnp.int64), 'W_in': w(ks[2], (IN, H), IN), 'b_in': jnp.zeros((H,), jnp.float32), 'router_W': w(ks[3], (L, 2 * H, NE), 2 * H), 'router_b': jnp.zeros((L, NE), jnp.float32), 'weak_W': w(ks[4], (L, NW, H, H), H), 'weak_b': jnp.zeros((L, NW, H), jnp.float32), 'strong_W1': w(ks[5], (L, NS, H, 2 * H), H), 'strong_b1': jnp.zeros((L, NS, 2 * H), jnp.float32), 'strong_W2': w(ks[6], (L, NS, 2 * H, H), 2 * H), 'strong_b2': jnp.zeros((L, NS, H), jnp.float32), 'conf_W': w(ks[7], (L, H, 1), H), 'conf_b': jnp.zeros((L, 1), jnp.float32), 'W_out': w(ks[8], (H, OUT), H), 'b_out': jnp.zeros((OUT,), jnp.float32)}
        return inp
    _L1_gnn_all = _L1_gnn_setup()
    _L1_gnn_in = {k: v for k, v in _L1_gnn_all.items() if k in ('W_in', 'b_in', 'router_W', 'router_b', 'weak_W', 'weak_b', 'strong_W1', 'strong_b1', 'strong_W2', 'strong_b2', 'conf_W', 'conf_b', 'W_out', 'b_out')}
    del _L1_gnn_all
    return {'x': x, 'src': src, 'dst': dst, 'L0_gnn_W_l0': _L0_gnn_in['W_l0'], 'L0_gnn_b_l0': _L0_gnn_in['b_l0'], 'L0_gnn_W_r0': _L0_gnn_in['W_r0'], 'L0_gnn_W_l1': _L0_gnn_in['W_l1'], 'L0_gnn_b_l1': _L0_gnn_in['b_l1'], 'L0_gnn_W_r1': _L0_gnn_in['W_r1'], 'L1_gnn_W_in': _L1_gnn_in['W_in'], 'L1_gnn_b_in': _L1_gnn_in['b_in'], 'L1_gnn_router_W': _L1_gnn_in['router_W'], 'L1_gnn_router_b': _L1_gnn_in['router_b'], 'L1_gnn_weak_W': _L1_gnn_in['weak_W'], 'L1_gnn_weak_b': _L1_gnn_in['weak_b'], 'L1_gnn_strong_W1': _L1_gnn_in['strong_W1'], 'L1_gnn_strong_b1': _L1_gnn_in['strong_b1'], 'L1_gnn_strong_W2': _L1_gnn_in['strong_W2'], 'L1_gnn_strong_b2': _L1_gnn_in['strong_b2'], 'L1_gnn_conf_W': _L1_gnn_in['conf_W'], 'L1_gnn_conf_b': _L1_gnn_in['conf_b'], 'L1_gnn_W_out': _L1_gnn_in['W_out'], 'L1_gnn_b_out': _L1_gnn_in['b_out']}

def reference(x, src, dst, L0_gnn_W_l0, L0_gnn_b_l0, L0_gnn_W_r0, L0_gnn_W_l1, L0_gnn_b_l1, L0_gnn_W_r1, L1_gnn_W_in, L1_gnn_b_in, L1_gnn_router_W, L1_gnn_router_b, L1_gnn_weak_W, L1_gnn_weak_b, L1_gnn_strong_W1, L1_gnn_strong_b1, L1_gnn_strong_W2, L1_gnn_strong_b2, L1_gnn_conf_W, L1_gnn_conf_b, L1_gnn_W_out, L1_gnn_b_out):
    import jax
    import jax.numpy as jnp

    def _L0_gnn_ref(x, edge_index, W_l0, b_l0, W_r0, W_l1, b_l1, W_r1):
        import jax, jax.numpy as jnp
        import numpy as np
        N_NODES = 3125
        N_EDGES = 50000
        D_IN = 128
        D_HID = 128
        D_OUT = 128

        def _sage_conv(x, src, dst, W_l, b_l, W_r):
            msg = x[src]
            summed = jax.ops.segment_sum(msg, dst, num_segments=N_NODES)
            cnt = jax.ops.segment_sum(jnp.ones((src.shape[0],), x.dtype), dst, num_segments=N_NODES)
            aggr = summed / jnp.maximum(cnt, 1.0)[:, None]
            return aggr @ W_l + b_l + x @ W_r
        src, dst = (edge_index[0], edge_index[1])
        h = jax.nn.relu(_sage_conv(x, src, dst, W_l0, b_l0, W_r0))
        out = _sage_conv(h, src, dst, W_l1, b_l1, W_r1)
        return out

    def _L1_gnn_ref(x, edge_index, W_in, b_in, router_W, router_b, weak_W, weak_b, strong_W1, strong_b1, strong_W2, strong_b2, conf_W, conf_b, W_out, b_out):
        import jax, jax.numpy as jnp
        import numpy as np
        TOPK = 2
        N = x.shape[0]
        L = router_W.shape[0]
        src = edge_index[0]
        dst = edge_index[1]
        deg = jax.ops.segment_sum(jnp.ones(src.shape, x.dtype), dst, num_segments=N)
        deg = jnp.clip(deg, 1.0)[:, None]
        h = x @ W_in + b_in
        rows = jnp.arange(N)[:, None]
        for l in range(L):
            agg = jax.ops.segment_sum(h[src], dst, num_segments=N) / deg
            logits = jnp.concatenate([h, agg], axis=-1) @ router_W[l] + router_b[l]
            vals, idx = jax.lax.top_k(logits, TOPK)
            gates = jax.nn.softmax(vals, axis=-1)
            gate_dense = jnp.zeros_like(logits).at[rows, idx].set(gates)
            weak = jax.nn.relu(jnp.einsum('nh,ehf->nef', agg, weak_W[l]) + weak_b[l])
            sh = jax.nn.relu(jnp.einsum('nh,ehf->nef', agg, strong_W1[l]) + strong_b1[l])
            strong = jnp.einsum('nef,efh->neh', sh, strong_W2[l]) + strong_b2[l]
            experts = jnp.concatenate([weak, strong], axis=1)
            moe = jnp.einsum('ne,neh->nh', gate_dense, experts)
            conf = jax.nn.sigmoid(h @ conf_W[l] + conf_b[l])
            h = h + conf * moe
        return h @ W_out + b_out
    edge_index = jnp.stack([src, dst])
    x = _layernorm(x + _L0_gnn_ref(x, edge_index, L0_gnn_W_l0, L0_gnn_b_l0, L0_gnn_W_r0, L0_gnn_W_l1, L0_gnn_b_l1, L0_gnn_W_r1), axis=-1)
    x = _layernorm(x + _L1_gnn_ref(x, edge_index, L1_gnn_W_in, L1_gnn_b_in, L1_gnn_router_W, L1_gnn_router_b, L1_gnn_weak_W, L1_gnn_weak_b, L1_gnn_strong_W1, L1_gnn_strong_b1, L1_gnn_strong_W2, L1_gnn_strong_b2, L1_gnn_conf_W, L1_gnn_conf_b, L1_gnn_W_out, L1_gnn_b_out), axis=-1)
    return x

_drawn_inputs = setup_inputs


def setup_inputs(seed=0):
    import zlib

    import numpy as np

    out = dict(_drawn_inputs(seed))
    spreads = {'L0_gnn_b_l0': (0.0, 0.1),
     'L0_gnn_b_l1': (0.0, 0.1),
     'L1_gnn_b_in': (0.0, 0.1),
     'L1_gnn_router_b': (0.0, 0.1),
     'L1_gnn_weak_b': (0.0, 0.31),
     'L1_gnn_strong_b1': (0.0, 0.29),
     'L1_gnn_strong_b2': (0.0, 0.1),
     'L1_gnn_conf_b': (0.0, 0.8),
     'L1_gnn_b_out': (0.0, 0.1)}
    factors = {}
    for name, (base, spread) in spreads.items():
        noise = np.random.default_rng([zlib.crc32(name.encode()), seed]).standard_normal(out[name].shape)
        drawn = base * np.exp(spread * noise) if base else spread * noise
        out[name] = jnp.asarray(drawn.astype(out[name].dtype))
    for name, factor in factors.items():
        out[name] = (out[name] * factor).astype(out[name].dtype)
    return out
```

```python
from contextlib import ExitStack

import concourse.bass as bass
from concourse import mybir
from concourse.alu_op_type import AluOpType as ALU

ACT = mybir.ActivationFunctionType
F32 = mybir.dt.float32
BF16 = mybir.dt.bfloat16
I32 = mybir.dt.int32
U32 = mybir.dt.uint32
EPE = mybir.EngineType.PE
EDVE = mybir.EngineType.DVE
EPOOL = mybir.EngineType.Pool
EACT = mybir.EngineType.Activation

P = 128
N = 3125
E = 100000
S = 25
CE = 125
C = E // CE
CP = 100
CJ = C // CP
W = 4
NW = S * P // W
WC = W * S
T = C + NW
G = 4
B16 = 16
RS = 16
NOH = 4
TP = 400
ABSENT_DST = 8000

NB = 5
TB = S // NB
BN = TB * P
HN = BN // 2
NK = 5
SK = S // NK
D = 128
H = 256
NL = 3
NE = 8
NS = 4
FT = 512 // P
GROUPS = ((0, 3), (3, 5))
LN_EPS = 1e-5

ACT_ITEMS = (2, 2, 38, 36, 40)
DVE_ITEMS = (2, 2, 48, 40, 42)
AGG_BANKS = (4, 2, 3, 5, 5)
ACT_STATS = (0, 1, 1, 1, 2)
SUMMED = (4, 2, 2, 4, 4)
WEAK_BANKS = (6, 7, 1, 2, 3)
DVE_STEPS = (9, 10, 44, 44, 46)


def before(counts, p):
    return NB * sum(counts[:p])


def build(nc, x, src, dst, Wl0, bl0, Wr0, Wl1, bl1, Wr1, W_in, b_in, router_W, router_b, weak_W, weak_b,
          strong_W1, strong_b1, strong_W2, strong_b2, conf_W, conf_b, W_out, b_out, out):
    with ExitStack() as ctx:
        def sb(name, shape, dt):
            return ctx.enter_context(nc.sbuf_tensor(name, shape, dt))

        def sem(name):
            return ctx.enter_context(nc.semaphore(name))

        def dram(name, shape, dt):
            return nc.dram_tensor(name, shape, dt, kind="Internal").ap()

        psum = ctx.enter_context(nc.psum_tensor("psum", [P, 8, 512], F32))

        adj_d = dram("adj_d", [P, NB * NK, SK * BN], BF16)
        split_d = dram("split_d", [P, S, 3, H], BF16)
        x_d = dram("x_d", [P, S, D], F32)
        h1_d = dram("h1_d", [P, S, D], F32)
        x1_d = dram("x1_d", [P, S, D], F32)
        h_d = dram("h_d", [P, S, H], F32)

        arena = sb("arena", [P, 103900], BF16)
        used = [0, P]

        def carve(shape, dt, rows=P):
            n = 1
            for k in shape:
                n *= k
            cols = n * (1 if dt == BF16 else 2)
            a = arena[0:rows, used[0]:used[0] + cols]
            used[0] += cols
            assert used[0] <= 103900, used[0]
            a = a if dt == BF16 else a.bitcast(dt)
            names = "abcd"[:len(shape)]
            if len(shape) > 1:
                a = a.rearrange(f"p ({' '.join(names)}) -> p {' '.join(names)}", **dict(zip(names[1:], shape[1:])))
            return a

        adj = carve([NW * WC], BF16)
        build_from = used[0]
        ones_b = carve([512], BF16)
        zeros_b = carve([512], BF16)
        iota2 = carve([P, 2], BF16)
        lo_of = carve([T], BF16, CE)
        loc_of = carve([T], BF16, CE)
        w_off = carve([T // G], I32, 1)
        w_rel = carve([T // G * (G - 1)], I32, 1)
        oh1 = carve([NOH, B16 // 2, P, 2], BF16, CE)
        wf = oh1[0:1].rearrange("p b n c z -> p (b n c z)")[:, 0:2 * T].bitcast(F32)
        first_w = carve([8, WC], BF16)
        tables_from = used[0]
        step_no = carve([T], F32)
        wdiff = carve([TP], F32, CE)
        iota_f = carve([P], F32)
        used[0] = tables_from
        oh2 = carve([NOH, B16 // 2, WC, 2], BF16, CE)
        first = carve([4, CE], BF16, 1)
        last_w = carve([CJ], I32, CP)
        chunk_no = carve([CJ], I32, CP)
        chunk_end = carve([CJ], F32, CP)
        EK = 2 * CJ * CE * 2
        used[0] = NW * WC - (5 * EK + 2 * CJ * TP)
        tail_from = used[0]
        edge_src = carve([2, CJ, CE], I32, CP)
        edge_dst = carve([2, CJ, CE], I32, CP)
        key_a = carve([2, CJ, CE], I32, CP)
        key_b = carve([2, CJ, CE], I32, CP)
        delta = carve([4, CJ, CE], BF16, CP)
        past = carve([2, CJ, TP], BF16, CP)
        assert used[0] == NW * WC

        used[0] = build_from
        ring = carve([NK, SK, BN], BF16)
        x_all_from = used[0]
        x_all = carve([S, D], F32)
        used[0] = x_all_from
        aggx = carve([BN], F32)
        xT = carve([BN], F32)
        st = carve([TB, 3, H], BF16)
        assert used[0] <= x_all_from + 2 * S * D
        used[0] = 0
        hs = carve([S, 3, H], BF16)
        w1 = carve([NS, 2, 512], F32)
        w2 = carve([NS, FT, H], F32)
        wk = carve([NS, 2, H], F32)
        wkb = carve([NS, H], F32)
        b2b = carve([NS, H], F32)
        recip = carve([S * P], F32)
        has_in = carve([S * P], BF16)
        hblk = carve([TB, H], F32)
        rblk = carve([TB, D], F32)
        hT = carve([2, BN], F32)
        aggT = carve([2, BN], F32)
        sh0 = carve([FT, BN], F32)
        sh1 = carve([FT, BN], F32)
        sh = (sh0, sh1)
        tmp = carve([TB, H], F32)
        wl = [carve([D], F32) for _ in range(2)]
        wr = [carve([D], F32) for _ in range(2)]
        w_in = carve([H], F32)
        w_out = carve([2, D], F32)
        bl = [carve([D], F32) for _ in range(2)]
        b_outb = carve([D], F32)
        b_inb = carve([H], F32)
        assert used[0] <= build_from, used[0]

        ones_s = sb("ones_s", [P, P], BF16)
        ident = sb("ident", [P, P], F32)
        part_no = sb("part_no", [P, 1], F32)
        eno = sb("eno", [P, NE], F32)
        rw = sb("rw", [P, NL, 4, NE + 1], F32)
        rbias = sb("rbias", [P, NL, NE + 1], F32)
        b1c = sb("b1c", [P, NL, NS * FT], F32)
        binc = sb("binc", [P, 2], F32)
        lg = sb("lg", [P, TB, 16], F32)
        mx = sb("mx", [P, TB, 8], F32)
        ix = sb("ix", [P, TB, 8], U32)
        ixf = sb("ixf", [P, TB, 2], F32)
        ex = sb("ex", [P, 2, TB], F32)
        ee = sb("ee", [P, 2, TB], F32)
        rr = sb("rr", [P, 2, TB], F32)
        g12 = sb("g12", [P, 2, TB], F32)
        gt = sb("gt", [P, TB, NE], F32)
        gu = sb("gu", [P, TB, NE], F32)
        bs = sb("bs", [P, TB, 6], F32)
        ba = sb("ba", [P, TB, 2], F32)

        s_in = sem("edges_in"); s_const = sem("constants"); s_v = sem("vector_steps"); s_past = sem("chunks_past")
        s_gath = sem("keys_gathered"); s_tab = sem("offsets_ready"); s_lo = sem("sources_ready"); s_pad = sem("edges_padded")
        s_gread = sem("keys_read")
        s_oh1 = sem("source_one_hots"); s_oh2 = sem("window_one_hots"); s_step = sem("superstep_summed")
        s_wide = sem("new_windows_copied"); s_first = sem("first_window_added"); s_zero = sem("adjacency_zeroed")
        s_rel = [sem(f"piece_laid_out_{k}") for k in range(NK)]
        s_dump = [sem(f"piece_stored_{k}") for k in range(NK)]
        s_x = sem("x_in"); s_xpad = sem("x_padded"); s_xst = sem("x_stored"); s_xsp = sem("x_split")
        s_wt = sem("weights_in"); s_bias = sem("expert_biases_in")
        s_w = [sem(f"strong_weights_in_{e}") for e in range(NS)]
        s_wk = [sem(f"weak_weights_in_{e}") for e in range(NS)]
        s_ring = [sem(f"piece_in_{k}") for k in range(NK)]
        s_piece = sem("pieces_used")
        s_hs = [sem(f"splits_in_{b}") for b in range(NB)]
        s_ldh = sem("h_block_in"); s_ldr = sem("residual_block_in")
        s_agg = sem("banks_aggregated"); s_aggf = sem("aggregates_taken")
        s_ta = sem("items_for_scalar"); s_fa = sem("items_taken_by_scalar")
        s_td = sem("items_for_vector"); s_fd = sem("items_taken_by_vector")
        s_ex = sem("statistics_for_scalar"); s_exd = sem("statistics_from_scalar")
        s_res = sem("block_done"); s_split = sem("block_split")
        s_sst = sem("block_stored"); s_hst = sem("splits_stored")
        s_prep = sem("tables_ready")

        block = ctx.enter_context(nc.Block())

        LJ = (CJ - 1) * CP * CE

        def at(counts, p, b, k):
            return b * counts[p] + (before(counts, p) + k)

        def half(a, h):
            return a[:, h * HN:(h + 1) * HN]

        def tile(a, t):
            return a[:, t * P:(t + 1) * P]

        def strong_items(p, e):
            return (8 if p == 2 else 0) + (TB * e if e < NS - 1 else TB * (NS - 1 + NS))

        def weak_items(p, e):
            return (8 if p == 2 else 0) + TB * (NS - 1 + e)

        def sh_items(p, e):
            return (6 if p == 2 else 4) + 2 * FT * e

        def layout(eng, copy, ks):
            view = adj.rearrange("p (w s d) -> p s w d", s=S, d=W)
            NWB = BN // W

            def block_pieces(b, head=False):
                for k in ks:
                    if not head:
                        eng.wait_ge(s_dump[k], b * 16)
                    for s in range(SK):
                        ins = copy(ring[:, k, s].rearrange("p (w d) -> p w d", d=W),
                                   view[:, k * SK + s, bass.ds(b * NWB, NWB)])
                    ins.then_inc(s_rel[k], 1)
            block_pieces(0, head=True)
            with eng.Fori(1, NB) as b:
                block_pieces(b)

        @block.sync
        def _(sp):
            sp.wait_ge(s_pad, 2)
            for a, b in ((edge_src, src), (edge_dst, dst)):
                sp.dma_start(a[:, 0], b.rearrange("(j p e) -> p j e", p=CP, e=CE)).then_inc(s_in, 16)
                sp.dma_start(a[:, 1, 0:CJ - 1], b[CE:CE + LJ].rearrange("(j p e) -> p j e", p=CP, e=CE)).then_inc(s_in, 16)
                sp.dma_start(a[0:CP - 1, 1, CJ - 1], b[CE + LJ:E].rearrange("(p e) -> p e", e=CE)).then_inc(s_in, 16)
            for l in range(NL):
                for kt in range(4):
                    sp.dma_start(rw[:, l, kt, 0:NE], router_W[l, kt * P:(kt + 1) * P]).then_inc(s_wt, 16)
                for kt in range(2):
                    sp.dma_start(rw[:, l, kt, NE:NE + 1], conf_W[l, kt * P:(kt + 1) * P]).then_inc(s_wt, 16)
                sp.dma_start(rbias[:, l, 0:NE], router_b[l:l + 1].broadcast_to((P, NE))).then_inc(s_wt, 16)
                sp.dma_start(rbias[:, l, NE:NE + 1], conf_b[l:l + 1].broadcast_to((P, 1))).then_inc(s_wt, 16)
                for e in range(NS):
                    sp.dma_start(b1c[:, l, e * FT:(e + 1) * FT], strong_b1[l, e].rearrange("(f p) -> p f", p=P), allow_slow_non_contiguous=True).then_inc(s_wt, 16)
            sp.dma_start(binc[:, :], b_in.rearrange("(f p) -> p f", p=P), allow_slow_non_contiguous=True).then_inc(s_wt, 16)
            sp.wait_ge(s_xpad, 1)
            sp.dma_start(x_all[:, 0:S - 1], x[0:(S - 1) * P].rearrange("(t p) d -> p t d", p=P)).then_inc(s_x, 16)
            sp.dma_start(x_all[0:N - (S - 1) * P, S - 1], x[(S - 1) * P:N]).then_inc(s_x, 16)
            with sp.Fori(0, NB) as b:
                for k in range(NK):
                    sp.wait_ge(s_rel[k], b + 1)
                    sp.dma_start(adj_d[:, bass.ds(b * NK + k, 1)].rearrange("p o n -> p (o n)"), ring[:, k].rearrange("p s n -> p (s n)")).then_inc(s_dump[k], 16)
            sp.wait_ge(s_x, 32)
            sp.dma_start(x_d, x_all).then_inc(s_xst, 16)
            for k in range(NK):
                sp.wait_ge(s_dump[k], 16 * NB)

            for o, i in ((wl[0], Wl0), (wr[0], Wr0), (wl[1], Wl1), (wr[1], Wr1), (w_in, W_in)):
                sp.dma_start(o, i).then_inc(s_wt, 16)
            sp.dma_start(w_out, W_out.rearrange("(k p) d -> p k d", p=P)).then_inc(s_wt, 16)
            for o, i in ((bl[0], bl0), (bl[1], bl1), (b_outb, b_out), (b_inb, b_in)):
                sp.dma_start(o, i.unsqueeze(0).broadcast_to((P, i.shape[0]))).then_inc(s_wt, 16)

            def expert_weights(l, p):
                for e in range(NS - 1):
                    if l:
                        sp.wait_ge(s_td, at(DVE_ITEMS, p - 1, NB - 1, strong_items(p - 1, e) + TB))
                    strong(l, e)
                for e in range(NS):
                    if l:
                        sp.wait_ge(s_td, at(DVE_ITEMS, p - 1, NB - 1, weak_items(p - 1, e) + TB))
                    sp.dma_start(wk[:, e], weak_W[l, e].rearrange("(k p) f -> p k f", p=P)).then_inc(s_wk[e], 16)
                if l:
                    sp.wait_ge(s_td, at(DVE_ITEMS, p - 1, NB - 1, strong_items(p - 1, NS - 1) + TB))
                strong(l, NS - 1)
                if l:
                    sp.wait_ge(s_res, NB * p)
                sp.dma_start(wkb, weak_b[l:l + 1].broadcast_to((P, NS, H))).then_inc(s_bias, 16)
                sp.dma_start(b2b, strong_b2[l:l + 1].broadcast_to((P, NS, H))).then_inc(s_bias, 16)

            def strong(l, e):
                sp.dma_start(w1[:, e], strong_W1[l, e].rearrange("(k p) f -> p k f", p=P)).then_inc(s_w[e], 16)
                sp.dma_start(w2[:, e], strong_W2[l, e].rearrange("(k p) f -> p k f", p=P)).then_inc(s_w[e], 16)

            def pieces(p, b, head=False):
                for k in range(NK):
                    if not head and k < NK - 1:
                        sp.wait_ge(s_piece, (b + NB * p - 1) * (NK - 1) + k + 1)
                    elif not head:
                        sp.wait_ge(s_agg, at(AGG_BANKS, p, b, 0) - (AGG_BANKS[p] - SUMMED[p]) if not isinstance(b, int) or b
                                   else before(AGG_BANKS, p) - (AGG_BANKS[p - 1] - SUMMED[p - 1]))
                    sp.dma_start(ring[:, k].rearrange("p s n -> p (s n)"), adj_d[:, bass.ds(b * NK + k, 1)].rearrange("p o n -> p (o n)")).then_inc(s_ring[k], 16)

            def states(p, b, head=False):
                if not head:
                    sp.wait_ge(s_sst, (b + NB * p) * 16)
                    if p < 4:
                        sp.wait_ge(s_hst, (b + NB * p) * 16)
                if p in (1, 3, 4):
                    o, i = (hblk[:, :, 0:D], h1_d) if p == 1 else (hblk, h_d)
                    sp.dma_start(o, i[:, bass.ds(b * TB, TB)]).then_inc(s_ldh, 16)
                if p != 3:
                    i = x_d if p < 2 else x1_d
                    sp.dma_start(rblk, i[:, bass.ds(b * TB, TB)]).then_inc(s_ldr, 16)

            for p in range(5):
                pieces(p, 0, head=(p == 0))
                if p:
                    sp.wait_ge(s_agg, before(AGG_BANKS, p) - (AGG_BANKS[p - 1] - SUMMED[p - 1]))
                    for b in range(NB):
                        if p < 3 or b < NB - 1:
                            sp.wait_ge(s_hst, 16 * (NB * (p - 1) + b + 1))
                            w = D if p < 3 else H
                            sp.dma_start(hs[:, b * TB:(b + 1) * TB, :, 0:w].rearrange("p t k d -> p (t k) d"),
                                         split_d[:, b * TB:(b + 1) * TB, :, 0:w].rearrange("p t k d -> p (t k) d")).then_inc(s_hs[b], 16)
                else:
                    sp.wait_ge(s_xst, 16)
                if p > 2:
                    expert_weights(p - 2, p)
                    sp.wait_ge(s_hst, 16 * (NB * (p - 1) + NB))
                    sp.dma_start(hs[:, (NB - 1) * TB:S], split_d[:, (NB - 1) * TB:S]).then_inc(s_hs[NB - 1], 16)
                states(p, 0, head=(p == 0))
                if p == 0:
                    expert_weights(0, 0)
                with sp.Fori(1, NB) as b:
                    pieces(p, b)
                    states(p, b)
            sp.wait_ge(s_sst, 16 * (NB * 5 + 1))

        @block.gpsimd
        def _(pool):
            pool.nop().then_inc(s_first, 1)
            pool.memset(edge_src[:, 1], 0).then_inc(s_pad, 1)
            pool.memset(edge_dst[:, 1], ABSENT_DST).then_inc(s_pad, 1)
            pool.iota(chunk_no[:, :], [[CP, CJ]], base=0, channel_multiplier=1).then_inc(s_const, 1)
            pool.iota(step_no[:, :], [[1, T]], base=0, channel_multiplier=0, allow_small_or_imprecise_dtypes=True).then_inc(s_const, 1)
            pool.iota(iota2[:, :, :], [[1, P], [0, 2]], base=0, channel_multiplier=0, allow_small_or_imprecise_dtypes=True).then_inc(s_const, 1)
            pool.iota(iota_f[:, :], [[1, P]], base=0, channel_multiplier=0, allow_small_or_imprecise_dtypes=True).then_inc(s_const, 1)
            pool.memset(ones_b[:, :], 1.0).then_inc(s_const, 1)
            pool.iota(part_no[:, :], [[0, 1]], base=0, channel_multiplier=1, allow_small_or_imprecise_dtypes=True).then_inc(s_const, 1)
            pool.memset(zeros_b[:, :], 0.0).then_inc(s_const, 1)
            pool.memset(adj[:, 0:tail_from].bitcast(I32), 0).then_inc(s_zero, 1)
            pool.wait_ge(s_gath, T // TP)
            pool.memset(adj[:, tail_from:NW * WC].bitcast(I32), 0).then_inc(s_zero, 1)
            pool.wait_ge(s_zero, 2)
            pool.wait_ge(s_tab, 1)

            def adds(i):
                _, off = nc.values_load_multi_w_load_instructions(
                    w_off[0:1, bass.ds(i * RS, RS)], engines=(EPOOL,), min_val=0, max_val=(NW - G) * WC,
                    skip_runtime_bounds_check_because="a window's offset")
                for u in range(RS):
                    pool.wait_ge(s_wide, i * RS + u + 2)
                    pool.wait_ge(s_first, i * RS + u + 1)
                    a = adj[:, bass.ds(off[u], WC)]
                    pool.tensor_tensor(a, first_w[:, u % 8], a, ALU.add).then_inc(s_first, 1)
            with pool.Fori(0, T // G // RS) as i:
                adds(i)
            pool.memset(ones_s[:, :], 1.0).then_inc(s_prep, 1)
            pool.iota(eno[:, :], [[1, NE]], base=0, channel_multiplier=0, allow_small_or_imprecise_dtypes=True).then_inc(s_prep, 1)
            for l in range(NL):
                pool.memset(rw[:, l, 2:4, NE:NE + 1], 0.0).then_inc(s_prep, 1)
            pool.wait_ge(s_first, T // G + 1)
            pool.wait_ge(s_wide, T // G + 1)
            pool.memset(x_all[:, S - 1], 0.0).then_inc(s_xpad, 1)

            for p in range(5):
                def stores(b, last=False):
                    pool.wait_ge(s_res, b + NB * p + 1)
                    if p < 4:
                        o, i = ((h1_d, hblk[:, :, 0:D]), (x1_d, rblk), (h_d, hblk), (h_d, hblk))[p]
                        pool.dma_start(o[:, bass.ds(b * TB, TB)], i).then_inc(s_sst, 16)
                        pool.wait_ge(s_split, b + NB * p + 1)
                        w = D if p < 2 else H
                        pool.dma_start(split_d[:, bass.ds(b * TB, TB), :, 0:w].rearrange("p t k d -> p (t k) d"),
                                       st[:, :, :, 0:w].rearrange("p t k d -> p (t k) d")).then_inc(s_hst, 16)
                    elif not last:
                        pool.dma_start(out[bass.ds(b * BN, BN)].rearrange("(t p) d -> p t d", p=P), rblk).then_inc(s_sst, 16)
                    else:
                        n0 = (NB - 1) * BN
                        pool.dma_start(out[n0:(S - 1) * P].rearrange("(t p) d -> p t d", p=P), rblk[:, 0:TB - 1]).then_inc(s_sst, 16)
                        pool.dma_start(out[(S - 1) * P:N], rblk[0:N - (S - 1) * P, TB - 1]).then_inc(s_sst, 16)
                if p < 4:
                    with pool.Fori(0, NB) as b:
                        stores(b)
                else:
                    with pool.Fori(0, NB - 1) as b:
                        stores(b)
                    stores(NB - 1, last=True)

        @block.vector
        def _(v):
            v.nop().then_inc(s_aggf, 1)
            v.nop().then_inc(s_fd, 2)
            n = [0]

            def link(ins):
                n[0] += 1
                ins.then_inc(s_v, 1)
                v.wait_ge(s_v, n[0])
            v.wait_ge(s_in, 96)
            v.wait_ge(s_const, 7)
            link(v.tensor_scalar(ident[:, :], iota_f, part_no[:, 0:1], None, ALU.is_equal))
            link(v.tensor_scalar(key_a[:], edge_src[:], 127, None, ALU.bitwise_and))
            link(v.tensor_tensor(delta[:, 0], key_a[:, 1], key_a[:, 0], ALU.subtract))
            link(v.tensor_copy(first[:, 0], key_a[0:1, 0, 0]))
            link(v.tensor_scalar(key_a[:], edge_src[:], 7, 2, ALU.logical_shift_right, ALU.logical_shift_left))
            link(v.tensor_scalar(key_b[:], edge_dst[:], 3, None, ALU.bitwise_and))
            link(v.tensor_tensor(key_a[:], key_a[:], key_b[:], ALU.bitwise_or))
            link(v.tensor_tensor(delta[:, 1], key_a[:, 1], key_a[:, 0], ALU.subtract))
            link(v.tensor_copy(first[:, 1], key_a[0:1, 0, 0]))
            link(v.tensor_scalar(key_a[:], edge_dst[:], 5, 3, ALU.logical_shift_right, ALU.logical_shift_left))
            link(v.tensor_tensor(delta[:, 2], key_a[:, 1], key_a[:, 0], ALU.subtract))
            link(v.tensor_copy(first[:, 2], key_a[0:1, 0, 0]))
            link(v.tensor_scalar(key_a[:], edge_dst[:], 2, 7, ALU.logical_shift_right, ALU.bitwise_and))
            link(v.scalar_tensor_tensor(delta[:, 3], key_a[:, 1], 1.0, key_a[:, 0], ALU.add, ALU.subtract))
            link(v.tensor_copy(first[:, 3], key_a[0:1, 0, 0]))
            link(v.tensor_scalar(last_w[:, :], edge_dst[:, 0, :, CE - 1], 2, None, ALU.logical_shift_right))
            link(v.tensor_tensor(chunk_end[:, :], last_w[:, :], chunk_no[:, :], ALU.add))
            def compare(m):
                if m >= 2:
                    v.wait_ge(s_gath, m - 1)
                for j in range(CJ):
                    ins = v.tensor_scalar(past[:, m % 2, j], step_no[0:CP, m * TP:(m + 1) * TP], chunk_end[:, j:j + 1], None, ALU.is_gt)
                ins.then_inc(s_past, 1)

            compare(0)
            for m in range(T // TP):
                t0 = m * TP
                if m + 1 < T // TP:
                    compare(m + 1)
                v.wait_ge(s_gath, m + 1)
                h = 4 * (m % 2)
                link(v.tensor_tensor(wdiff[:, :], psum[0:CE, h, 0:TP], step_no[0:CE, t0:t0 + TP], ALU.subtract))
                link(v.scalar_tensor_tensor(wdiff[:, :], wdiff[:, :], float(WC), psum[0:CE, h + 1, 0:TP], ALU.mult, ALU.add))
                link(v.tensor_scalar(loc_of[:, t0:t0 + TP], wdiff[:, :], -1.0, float(P), ALU.max, ALU.min))
                link(v.scalar_tensor_tensor(wf[:, t0:t0 + TP], psum[0:1, h + 3, 0:TP], -1.0, step_no[0:1, t0:t0 + TP], ALU.mult, ALU.add))
                v.nop().then_inc(s_gread, 1)
            w4 = wf[:, :].rearrange("o (s g) -> o s g", g=G)
            link(v.tensor_scalar(w_off[:, :], w4[:, :, 0], float(WC), None, ALU.mult))
            link(v.tensor_tensor(w_rel[:, :].rearrange("o (s g) -> o s g", g=G - 1), w4[:, :, 1:G], w4[:, :, 0:1].broadcast_to((1, T // G, G - 1)), ALU.subtract))
            v.tensor_scalar(w_rel[:, :], w_rel[:, :], float(WC), None, ALU.mult).then_inc(s_tab, 1)
            v.wait_ge(s_zero, 2)
            v.wait_ge(s_tab, 1)

            k = B16 // G

            def one_hots(i, q):
                for oh, keys, cols, ready in ((oh2, loc_of, WC, s_oh2), (oh1, lo_of, P, s_oh1)):
                    shape = (CE, B16 // 2, cols, 2)
                    every = iota2[0:CE, 0:cols].unsqueeze(1).broadcast_to(shape)
                    key = keys[:, bass.ds(i * (NOH * B16) + q * B16, B16)].rearrange("p (n o z) -> p n o z", z=2, o=1).broadcast_to(shape)
                    v.tensor_tensor(oh[:, q], every, key, ALU.is_equal).then_inc(ready, 1)

            def batches(i, head=False):
                for q in range(NOH):
                    if not head:
                        v.wait_ge(s_step, i * (NOH * k) + (q + 1 - NOH) * k)
                    one_hots(i, q)
            v.wait_ge(s_lo, T // TP)
            batches(0, head=True)
            with v.Fori(1, T // B16 // NOH) as i:
                batches(i)
            v.wait_ge(s_first, T // G + 1)
            v.wait_ge(s_wide, T // G + 1)
            layout(v, v.tensor_copy, (0, 2, 4))
            v.wait_ge(s_x, 32)
            for k in range(NK):
                v.wait_ge(s_dump[k], 16 * NB)
            rest = sh0.rearrange("p f n -> p (f n)").rearrange("p (t d) -> p t d", d=D)
            for t0, t1 in ((0, 20), (20, 25)):
                xs = x_all[:, t0:t1]
                r = rest[:, 0:t1 - t0]
                link(v.tensor_copy(hs[:, t0:t1, 0, 0:D], xs))
                link(v.tensor_tensor(r, xs, hs[:, t0:t1, 0, 0:D], ALU.subtract))
                link(v.tensor_copy(hs[:, t0:t1, 1, 0:D], r))
                link(v.tensor_tensor(hs[:, t0:t1, 2, 0:D], r, hs[:, t0:t1, 1, 0:D], ALU.subtract))
            v.wait_ge(s_xst, 16)
            v.nop().then_inc(s_xsp, 1)
            v.wait_ge(s_wt, 16 * (NL * (8 + NS) + 1 + 10))
            v.wait_ge(s_prep, 2 + NL)
            started = n[0]

            for p in range(5):
                l = p - 2

                def one_block(b):
                    steps = [0]

                    def do(ins):
                        steps[0] += 1
                        ins.then_inc(s_v, 1)
                        v.wait_ge(s_v, at(DVE_STEPS, p, b, started + steps[0]))

                    def item(k):
                        v.wait_ge(s_td, at(DVE_ITEMS, p, b, k + 1))
                        return psum[:, 6 + k % 2]

                    def taken(ins):
                        ins.then_inc(s_fd, 1)

                    here = bass.ds(b * BN, BN)
                    if p == 0:
                        v.wait_ge(s_agg, at(AGG_BANKS, p, b, 2))
                        deg = tmp.rearrange("p t d -> p (t d)")
                        for h in range(2):
                            there = bass.ds(b * BN + h * HN, HN)
                            do(v.tensor_scalar(deg[:, h * HN:(h + 1) * HN], psum[:, 2 + h, 0:HN], 1.0, None, ALU.max))
                            do(v.reciprocal(recip[:, there], deg[:, h * HN:(h + 1) * HN]))
                            v.tensor_scalar(has_in[:, there], psum[:, 2 + h, 0:HN], 1.0, None, ALU.min).then_inc(s_aggf, 1)
                    F = 2 if p > 2 else 1
                    to = aggx.unsqueeze(1) if p == 2 else aggT
                    for f in range(F):
                        for h in range(2):
                            q = 2 * f + h
                            v.wait_ge(s_agg, at(AGG_BANKS, p, b, (2 if p == 0 else 0) + q + 1))
                            v.tensor_tensor(half(to[:, f], h), psum[:, q, 0:HN], recip[:, bass.ds(b * BN + h * HN, HN)],
                                            ALU.mult).then_inc(s_aggf, 1)
                    if p < 2:
                        res = hblk[:, :, 0:D] if p == 0 else rblk
                        for k, (t0, t1) in enumerate(GROUPS):
                            u = tmp[:, t0:t1, 0:D]
                            v_in = item(k)[:, 0:(t1 - t0) * D].rearrange("p (t d) -> p t d", d=D)
                            taken(v.tensor_tensor(u, v_in, bl[p].unsqueeze(1).broadcast_to((P, t1 - t0, D)), ALU.add))
                        v.wait_ge(s_fd, at(DVE_ITEMS, p, b, 2 + 2))
                        if p == 0:
                            do(v.tensor_scalar(res, tmp[:, :, 0:D], 0.0, None, ALU.max))
                        else:
                            v.wait_ge(s_ldr, (b + NB + 1) * 16)
                            do(v.tensor_tensor(res, res, tmp[:, :, 0:D], ALU.add))
                            layernorm(b, do, 0)
                        v.nop().then_inc(s_res, 1)
                        split(res, D, do)
                        v.nop().then_inc(s_split, 1)
                        assert steps[0] == DVE_STEPS[p], (p, steps[0])
                        return

                    if p == 2:
                        for k in range(4):
                            f, h = k // 2, k % 2
                            taken(v.scalar_tensor_tensor(half(aggT[:, f], h), has_in[:, bass.ds(b * BN + h * HN, HN)],
                                                         binc[:, f:f + 1], item(k)[:, 0:HN], ALU.mult, ALU.add))
                        for k, (t0, t1) in enumerate(((0, 2), (2, 3), (3, 4), (4, 5))):
                            v_in = item(4 + k)[:, 0:(t1 - t0) * H].rearrange("p (t d) -> p t d", d=H)
                            taken(v.tensor_tensor(hblk[:, t0:t1], v_in, b_inb.unsqueeze(1).broadcast_to((P, t1 - t0, H)), ALU.add))
                        v.wait_ge(s_fd, at(DVE_ITEMS, p, b, 8 + 2))

                    v.wait_ge(s_agg, at(AGG_BANKS, p, b, AGG_BANKS[p]))
                    lp = psum[:, 0, 0:TB * 16].rearrange("p (t e) -> p t e", e=16)[:, :, 0:NE + 1]
                    v.tensor_tensor(lg[:, :, 0:NE + 1], lp, rbias[:, l:l + 1].broadcast_to((P, TB, NE + 1)), ALU.add).then_inc(s_aggf, 1)
                    v.wait_ge(s_aggf, at(AGG_BANKS, p, b, AGG_BANKS[p] + 1))
                    v.tensor_scalar(ex[:, 1], lg[:, :, NE], -1.0, 87.0, ALU.mult, ALU.min)
                    for t in range(TB):
                        ins = v.max(mx[:, t], lg[:, t, 0:NE])
                    do(ins)
                    v.tensor_tensor(ex[:, 0], mx[:, :, 1], mx[:, :, 0], ALU.subtract)
                    for t in range(TB):
                        ins = v.max_index(ix[:, t], mx[:, t], lg[:, t, 0:NE])
                    do(ins)
                    v.nop().then_inc(s_ex, 1)
                    do(v.tensor_copy(ixf[:, :, :], ix[:, :, 0:2]))
                    v.wait_ge(s_exd, at(ACT_STATS, p, b, 1))
                    do(v.tensor_scalar(rr[:, :, :], ee[:, :, :], 1.0, None, ALU.add))
                    do(v.reciprocal(rr[:, :, :], rr[:, :, :]))
                    do(v.tensor_tensor(g12[:, 0], rr[:, 0], rr[:, 1], ALU.mult))
                    do(v.tensor_tensor(g12[:, 1], g12[:, 0], ee[:, 0], ALU.mult))
                    wide = lambda a: a.unsqueeze(2).broadcast_to((P, TB, NE))
                    every = eno[:, :].unsqueeze(1).broadcast_to((P, TB, NE))
                    do(v.tensor_tensor(gt[:, :, :], every, wide(ixf[:, :, 0]), ALU.is_equal))
                    do(v.tensor_tensor(gu[:, :, :], every, wide(ixf[:, :, 1]), ALU.is_equal))
                    do(v.tensor_tensor(gt[:, :, :], gt[:, :, :], wide(g12[:, 0]), ALU.mult))
                    do(v.tensor_tensor(gu[:, :, :], gu[:, :, :], wide(g12[:, 1]), ALU.mult))
                    do(v.tensor_tensor(gt[:, :, :], gt[:, :, :], gu[:, :, :], ALU.add))

                    v.wait_ge(s_bias, 32 * (l + 1))

                    def strong(e):
                        for t in range(TB):
                            g = gt[:, t, NS + e:NS + e + 1]
                            do(v.scalar_tensor_tensor(hblk[:, t], b2b[:, e], g, hblk[:, t], ALU.mult, ALU.add))
                            k = strong_items(p, e) + t
                            taken(v.scalar_tensor_tensor(hblk[:, t], item(k)[:, 0:H], g, hblk[:, t], ALU.mult, ALU.add))
                        v.wait_ge(s_fd, at(DVE_ITEMS, p, b, k + 1 + 2))

                    def weak(e):
                        for t in range(TB):
                            k = weak_items(p, e) + t
                            v.wait_ge(s_td, at(DVE_ITEMS, p, b, k + 1))
                            taken(v.tensor_tensor(tmp[:, t], psum[:, WEAK_BANKS[t], 0:H], wkb[:, e], ALU.add))
                        v.wait_ge(s_fd, at(DVE_ITEMS, p, b, k + 1 + 2))
                        for t in range(TB):
                            ins = v.tensor_scalar(tmp[:, t], tmp[:, t], 0.0, gt[:, t, e:e + 1], ALU.max, ALU.mult)
                        do(ins)
                        do(v.tensor_tensor(hblk, hblk, tmp, ALU.add))

                    if p > 2:
                        v.wait_ge(s_ldh, (b + NB * (p - 2) + 1) * 16)
                        v.wait_ge(s_ta, at(ACT_ITEMS, p, b, 4))
                    for e in range(NS - 1):
                        strong(e)
                    for e in range(NS):
                        weak(e)
                    strong(NS - 1)
                    if p < 4:
                        v.nop().then_inc(s_res, 1)
                        split(hblk, H, do)
                        v.nop().then_inc(s_split, 1)
                    else:
                        v.nop().then_inc(s_split, 1)
                        for k, (t0, t1) in enumerate(GROUPS):
                            v_in = item(40 + k)[:, 0:(t1 - t0) * D].rearrange("p (t d) -> p t d", d=D)
                            taken(v.tensor_tensor(tmp[:, t0:t1, 0:D], v_in, b_outb.unsqueeze(1).broadcast_to((P, t1 - t0, D)), ALU.add))
                        v.wait_ge(s_fd, at(DVE_ITEMS, p, b, 42 + 2))
                        v.wait_ge(s_ldr, (b + NB * 3 + 1) * 16)
                        do(v.tensor_tensor(rblk, rblk, tmp[:, :, 0:D], ALU.add))
                        layernorm(b, do, 1)
                        v.nop().then_inc(s_res, 1)
                    assert steps[0] == DVE_STEPS[p], (p, steps[0])

                def split(r, width, do):
                    u = tmp[:, :, 0:width]
                    do(v.tensor_copy(st[:, :, 0, 0:width], r))
                    do(v.tensor_tensor(u, r, st[:, :, 0, 0:width], ALU.subtract))
                    do(v.tensor_copy(st[:, :, 1, 0:width], u))
                    do(v.tensor_tensor(st[:, :, 2, 0:width], u, st[:, :, 1, 0:width], ALU.subtract))

                def layernorm(b, do, k):
                    for t in range(TB):
                        ins = v.bn_stats(bs[:, t], rblk[:, t])
                    do(ins)
                    v.memset(ex[:, 1], LN_EPS)
                    for t in range(TB):
                        ins = v.bn_aggr(ba[:, t], bs[:, t])
                    do(ins)
                    do(v.tensor_tensor(ex[:, 0], ba[:, :, 1], ex[:, 1], ALU.add))
                    v.nop().then_inc(s_ex, 1)
                    v.wait_ge(s_exd, at(ACT_STATS, p, b, k + 1))
                    do(v.reciprocal(rr[:, 0], ee[:, 0]))
                    for t in range(TB):
                        ins = v.tensor_scalar(rblk[:, t], rblk[:, t], ba[:, t, 0:1], rr[:, 0, t:t + 1], ALU.subtract, ALU.mult)
                    do(ins)

                with v.Fori(0, NB) as b:
                    one_block(b)

        @block.scalar
        def _(act):
            act.nop().then_inc(s_wide, 1)
            for m in range(T // TP):
                act.wait_ge(s_gath, m + 1)
                act.copy(lo_of[:, m * TP:(m + 1) * TP], psum[0:CE, 4 * (m % 2) + 2, 0:TP]).then_inc(s_lo, 1)
            act.wait_ge(s_tab, 1)
            act.wait_ge(s_zero, 2)
            def supersteps(i, head=False):
                _, off = nc.values_load_multi_w_load_instructions(
                    w_off[0:1, bass.ds(i * RS, RS)], engines=(EACT,), min_val=0, max_val=(NW - G) * WC,
                    skip_runtime_bounds_check_because="a window's offset")
                for u in range(RS):
                    act.wait_ge(s_step, i * RS + u + 1)
                    if not head or u >= 8:
                        act.wait_ge(s_first, i * RS + u - 6)
                    act.copy(first_w[:, u % 8], psum[:, u % 8, 0:WC])
                    act.wait_ge(s_wide, i * RS + u + 1)
                    act.copy(adj[:, bass.ds(off[u] + WC, (G - 1) * WC)], psum[:, u % 8, WC:G * WC]).then_inc(s_wide, 1)
            supersteps(0, head=True)
            with act.Fori(1, T // G // RS) as i:
                supersteps(i)
            act.wait_ge(s_first, T // G + 1)
            act.wait_ge(s_wide, T // G + 1)
            layout(act, act.copy, (1, 3))
            act.wait_ge(s_xsp, 1)
            act.nop().then_inc(s_fa, 2)

            for p in range(5):
                l = p - 2

                def one_block(b):
                    def item(k):
                        act.wait_ge(s_ta, at(ACT_ITEMS, p, b, k + 1))
                        return psum[:, 4 + k % 2]

                    def turned(to, k):
                        for t0, t1 in GROUPS:
                            act.copy(to[:, t0 * P:t1 * P], item(k)[:, 0:(t1 - t0) * P]).then_inc(s_fa, 1)
                            k += 1

                    if p < 2:
                        turned(hT[:, 0], 0)
                        if p == 1:
                            act.wait_ge(s_ex, at(ACT_STATS, p, b, 1))
                            act.activation(ee[:, 0], ex[:, 0], ACT.Sqrt).then_inc(s_exd, 1)
                        return
                    if p == 2:
                        turned(xT, 0)
                        for f in range(2):
                            for h in range(2):
                                act.activation(half(hT[:, f], h), item(2 + 2 * f + h)[:, 0:HN], ACT.Identity,
                                               bias=binc[:, f:f + 1]).then_inc(s_fa, 1)
                    else:
                        for f in range(2):
                            turned(hT[:, f], 2 * f)
                    for e in range(NS):
                        for f in range(FT):
                            for h in range(2):
                                act.activation(half(sh[e % 2][:, f], h), item(sh_items(p, e) + 2 * f + h)[:, 0:HN], ACT.Relu,
                                               bias=b1c[:, l, e * FT + f:e * FT + f + 1]).then_inc(s_fa, 1)
                        if e == 0:
                            act.wait_ge(s_ex, at(ACT_STATS, p, b, 1))
                            act.activation(ee[:, :, :], ex[:, :, :], ACT.Exp).then_inc(s_exd, 1)
                    if p == 4:
                        for f in range(2):
                            turned(hT[:, f], 36 + 2 * f)
                        act.wait_ge(s_ex, at(ACT_STATS, p, b, 2))
                        act.activation(ee[:, 0], ex[:, 0], ACT.Sqrt).then_inc(s_exd, 1)

                with act.Fori(0, NB) as b:
                    one_block(b)

        @block.tensor
        def _(pe):
            for m in range(T // TP):
                pe.wait_ge(s_past, m + 1)
                if m >= 2:
                    pe.wait_ge(s_gread, m - 1)
                    pe.wait_ge(s_lo, m - 1)
                h = 4 * (m % 2)
                for o, keys in ((h, (2, 3)), (h + 1, (1,)), (h + 2, (0,))):
                    for k in keys:
                        pe.matmul(psum[0:CE, o, 0:TP], first[0:1, k], ones_b[0:1, 0:TP], start=(k == keys[0]), stop=False)
                        for j in range(CJ):
                            pe.matmul(psum[0:CE, o, 0:TP], delta[:, k, j], past[:, m % 2, j], start=False, stop=(j == CJ - 1 and k == keys[-1]))
                for j in range(CJ):
                    mm = pe.matmul(psum[0:1, h + 3, 0:TP], ones_b[0:CP, 0:1], past[:, m % 2, j], start=(j == 0), stop=(j == CJ - 1))
                mm.then_inc(s_gath, 1)
            pe.wait_ge(s_gread, T // TP)
            pe.wait_ge(s_lo, T // TP)
            pe.wait_ge(s_tab, 1)
            k = B16 // G
            def supersteps(i, head=False):
                for q in range(NOH):
                    if q % 2 == 0:
                        n = 2 * k * (G - 1)
                        _, rel = nc.values_load_multi_w_load_instructions(
                            w_rel[0:1, bass.ds(i * (NOH // 2 * n) + q // 2 * n, n)], engines=(EPE,), min_val=0, max_val=(G - 1) * WC,
                            skip_runtime_bounds_check_because="a window's offset in its superstep")
                    pe.wait_ge(s_oh1, i * NOH + q + 1)
                    pe.wait_ge(s_oh2, i * NOH + q + 1)
                    for g in range(k):
                        u = q * k + g
                        bank = psum[:, u % 8]
                        if not head or u >= 8:
                            pe.wait_ge(s_wide, i * (NOH * k) + u - 6)
                        pe.matmul(bank[:, WC:G * WC], zeros_b[:, 0:P], zeros_b[:, WC:G * WC], start=True, stop=False, skip_group_check=True)
                        for z in range(G):
                            cols = bass.ds(rel[(q % 2 * k + g) * (G - 1) + z - 1], WC) if z else slice(0, WC)
                            n = (g * G + z) // 2
                            mm = pe.matmul(bank[:, cols], oh1[:, q, n, :, z % 2], oh2[:, q, n, :, z % 2],
                                           start=(z == 0), stop=(z == G - 1), skip_group_check=True)
                        mm.then_inc(s_step, 1)
            supersteps(0, head=True)
            with pe.Fori(1, T // B16 // NOH) as i:
                supersteps(i)
            pe.wait_ge(s_xsp, 1)
            pe.wait_ge(s_wt, 16 * (NL * (8 + NS) + 1 + 10))
            pe.wait_ge(s_prep, 2 + NL)

            for p in range(5):
                l = p - 2
                F = 2 if p > 2 else 1

                def one_block(b):
                    def for_act(k):
                        pe.wait_ge(s_fa, at(ACT_ITEMS, p, b, k + 1))
                        return psum[:, 4 + k % 2]

                    def for_dve(k):
                        pe.wait_ge(s_fd, at(DVE_ITEMS, p, b, k + 1))
                        return psum[:, 6 + k % 2]

                    def turn(blk, k):
                        for t0, t1 in GROUPS:
                            bank = for_act(k)
                            for t in range(t0, t1):
                                mm = pe.transpose(bank[:, (t - t0) * P:(t - t0 + 1) * P], blk[:, t], ident[:, :])
                            mm.then_inc(s_ta, 1)
                            k += 1

                    def summed(k, q, s):
                        f, h = q // 2, q % 2
                        for part in range(3):
                            mm = pe.matmul(psum[:, q, 0:HN], hs[:, k * SK + s, part, f * P:(f + 1) * P], half(ring[:, k, s], h),
                                           start=(k == 0 and s == 0 and part == 0), stop=(k == NK - 1 and s == SK - 1 and part == 2))
                        return mm

                    def counted(k, h, s):
                        return pe.matmul(psum[:, 2 + h, 0:HN], ones_s[:, :], half(ring[:, k, s], h),
                                         start=(k == 0 and s == 0), stop=(k == NK - 1 and s == SK - 1))

                    pe.wait_ge(s_aggf, at(AGG_BANKS, p, b, 1))
                    for k in range(NK):
                        pe.wait_ge(s_ring[k], (b + NB * p + 1) * 16)
                        if p:
                            pe.wait_ge(s_hs[k], 16 * p)
                        if k < NK - 1:
                            for s in range(SK):
                                for q in range(2 * F):
                                    mm = summed(k, q, s)
                                if p == 0:
                                    for h in range(2):
                                        mm = counted(k, h, s)
                            mm.then_inc(s_piece, 1)
                        else:
                            if p == 0:
                                for h in range(2):
                                    for s in range(SK):
                                        mm = counted(k, h, s)
                                    mm.then_inc(s_agg, 1)
                            for q in range(2 * F):
                                for s in range(SK):
                                    mm = summed(k, q, s)
                                mm.then_inc(s_agg, 1)
                    if p == 1 or p > 2:
                        pe.wait_ge(s_ldh, (b + NB * max(p - 2, 0) + 1) * 16)
                    else:
                        pe.wait_ge(s_ldr, (b + NB * p + 1) * 16)
                    if p < 2:
                        turn(rblk if p == 0 else hblk[:, :, 0:D], 0)
                        pe.wait_ge(s_fa, at(ACT_ITEMS, p, b, 2 + 2))
                        pe.wait_ge(s_aggf, at(AGG_BANKS, p, b, AGG_BANKS[p] + 1))
                        for k, (t0, t1) in enumerate(GROUPS):
                            bank = for_dve(k)
                            for t in range(t0, t1):
                                o = tile(bank, t - t0)
                                pe.matmul(o, tile(hT[:, 0], t), wr[p], start=True, stop=False)
                                mm = pe.matmul(o, tile(aggT[:, 0], t), wl[p], start=False, stop=True)
                            mm.then_inc(s_td, 1)
                        return
                    if p == 2:
                        turn(rblk, 0)
                        pe.wait_ge(s_fa, at(ACT_ITEMS, p, b, 2 + 2))
                        for k in range(4):
                            f, h = k // 2, k % 2
                            bank = for_act(2 + k)
                            pe.matmul(bank[:, 0:HN], w_in[:, f * P:(f + 1) * P], half(xT, h), start=True, stop=True).then_inc(s_ta, 1)
                        pe.wait_ge(s_aggf, at(AGG_BANKS, p, b, 2 + 1))
                        for k in range(4):
                            f, h = k // 2, k % 2
                            bank = for_dve(k)
                            pe.matmul(bank[:, 0:HN], w_in[:, f * P:(f + 1) * P], half(aggx, h), start=True, stop=True).then_inc(s_td, 1)
                        for k, (t0, t1) in enumerate(((0, 2), (2, 3), (3, 4), (4, 5))):
                            bank = for_dve(4 + k)
                            for t in range(t0, t1):
                                mm = pe.matmul(bank[:, (t - t0) * H:(t - t0 + 1) * H], tile(xT, t), w_in, start=True, stop=True)
                            mm.then_inc(s_td, 1)
                        pe.wait_ge(s_fd, at(DVE_ITEMS, p, b, 4 + 2))
                        pe.wait_ge(s_fa, at(ACT_ITEMS, p, b, 6 + 2))
                    else:
                        for f in range(2):
                            turn(hblk[:, :, f * P:(f + 1) * P], 2 * f)
                        pe.wait_ge(s_fa, at(ACT_ITEMS, p, b, 4 + 2))
                        pe.wait_ge(s_aggf, at(AGG_BANKS, p, b, 4 + 1))
                    for t in range(TB):
                        for kt in range(4):
                            a = hT[:, kt] if kt < 2 else aggT[:, kt - 2]
                            mm = pe.matmul(psum[:, 0, t * 16:t * 16 + NE + 1], tile(a, t), rw[:, l, kt], start=(kt == 0), stop=(kt == 3))
                    mm.then_inc(s_agg, 1)

                    def hidden(e):
                        pe.wait_ge(s_w[e], 32 * (l + 1))
                        for f in range(FT):
                            for h in range(2):
                                bank = for_act(sh_items(p, e) + 2 * f + h)
                                for kt in range(2):
                                    mm = pe.matmul(bank[:, 0:HN], w1[:, e, kt, f * P:(f + 1) * P], half(aggT[:, kt], h),
                                                   start=(kt == 0), stop=(kt == 1))
                                mm.then_inc(s_ta, 1)

                    def strong(e):
                        pe.wait_ge(s_fa, at(ACT_ITEMS, p, b, sh_items(p, e + 1) + 2))
                        for t in range(TB):
                            k = strong_items(p, e) + t
                            if e == NS - 1 and t < 2:
                                pe.wait_ge(s_fd, at(DVE_ITEMS, p, b, weak_items(p, NS - 1) + 2 + 2))
                                bank = psum[:, 6 + k % 2]
                            else:
                                bank = for_dve(k)
                            for f in range(FT):
                                mm = pe.matmul(bank[:, 0:H], tile(sh[e % 2][:, f], t), w2[:, e, f], start=(f == 0), stop=(f == FT - 1))
                            mm.then_inc(s_td, 1)

                    def weak(e):
                        pe.wait_ge(s_wk[e], 16 * (l + 1))
                        for t in range(TB):
                            k = weak_items(p, e) + t
                            if e or t < 2:
                                pe.wait_ge(s_fd, at(DVE_ITEMS, p, b, k - 2 if e else k + 2))
                            bank = psum[:, WEAK_BANKS[t]]
                            for kt in range(2):
                                mm = pe.matmul(bank[:, 0:H], tile(aggT[:, kt], t), wk[:, e, kt], start=(kt == 0), stop=(kt == 1))
                            mm.then_inc(s_td, 1)

                    hidden(0)
                    for e in range(1, NS):
                        hidden(e)
                        strong(e - 1)
                    for e in range(NS):
                        weak(e)
                    strong(NS - 1)
                    if p == 4:
                        pe.wait_ge(s_split, b + NB * 4 + 1)
                        for f in range(2):
                            turn(hblk[:, :, f * P:(f + 1) * P], 36 + 2 * f)
                        pe.wait_ge(s_fa, at(ACT_ITEMS, p, b, 40 + 2))
                        for k, (t0, t1) in enumerate(GROUPS):
                            bank = for_dve(40 + k)
                            for t in range(t0, t1):
                                for f in range(2):
                                    mm = pe.matmul(tile(bank, t - t0), tile(hT[:, f], t), w_out[:, f], start=(f == 0), stop=(f == 1))
                            mm.then_inc(s_td, 1)

                with pe.Fori(0, NB) as b:
                    one_block(b)


_INS = ['x', 'src', 'dst', 'L0_gnn_W_l0', 'L0_gnn_b_l0', 'L0_gnn_W_r0', 'L0_gnn_W_l1', 'L0_gnn_b_l1', 'L0_gnn_W_r1',
        'L1_gnn_W_in', 'L1_gnn_b_in', 'L1_gnn_router_W', 'L1_gnn_router_b', 'L1_gnn_weak_W', 'L1_gnn_weak_b',
        'L1_gnn_strong_W1', 'L1_gnn_strong_b1', 'L1_gnn_strong_W2', 'L1_gnn_strong_b2', 'L1_gnn_conf_W', 'L1_gnn_conf_b',
        'L1_gnn_W_out', 'L1_gnn_b_out']


def kernel(**inputs):
    import numpy as _np
    import concourse.bacc as _bacc
    from concourse import mybir as _mybir
    from concourse.bass_utils import run_bass_kernel_spmd as _run

    nc = _bacc.Bacc("TRN2", target_bir_lowering=False, num_devices=1)
    arrays, args = {}, []
    for name in _INS:
        a = _np.ascontiguousarray(inputs[name])
        arrays[f"in_{name}"] = a
        args.append(nc.dram_tensor(f"in_{name}", a.shape, _mybir.dt.from_np(a.dtype), kind="ExternalInput").ap())
    args.append(nc.dram_tensor("out_0", (N, D), _mybir.dt.float32, kind="ExternalOutput").ap())
    build(nc, *args)
    r = _run(nc, [arrays], core_ids=[0])
    return r.results[0]["out_0"]
```
